# Optimizing a Trainium2 kernel written in Bass

```python
import numpy as np
import jax
import jax.numpy as jnp

def _softmax(x, axis=-1):
    return jax.nn.softmax(x, axis=axis)

def _gelu(x):
    return jax.nn.gelu(x, approximate=True)

def _silu(x):
    return jax.nn.silu(x)

def _sigmoid(x):
    return jax.nn.sigmoid(x)

def _layernorm(x, axis=-1, eps=1e-05):
    m = jnp.mean(x, axis=axis, keepdims=True)
    v = jnp.var(x, axis=axis, keepdims=True)
    return (x - m) / jnp.sqrt(v + eps)

def _scatter_add(tgt, idx, src, axis=0):
    return tgt.at[idx].add(src)

def _segment_sum(src, seg, n):
    return jax.ops.segment_sum(src, seg, n)
kernel_name = 'mk_xattn_ffn_d1_seqx_r2_679473'

def setup_inputs(seed: int=0):
    np.random.seed(seed)
    _w = jnp.asarray

    def _rec_inputs():
        import jax
        import jax.numpy as jnp
        _rk = jax.random.key(seed)
        x = -0.0003929 + 0.9999 * jax.random.normal(jax.random.fold_in(_rk, 1), (32, 512, 512), jnp.float32)
        _lenS = 512 - jax.random.randint(jax.random.fold_in(_rk, 7), (32,), 0, max(1, 512 // 4) + 1, jnp.int32)
        _lenS2 = 512 - jax.random.randint(jax.random.fold_in(_rk, 8), (32,), 0, max(1, 512 // 4) + 1, jnp.int32)
        _ctx_1024P = jax.random.normal(jax.random.fold_in(_rk, 11), (32, 16, 512), jnp.float32)
        _ctx_1024c = jax.random.dirichlet(jax.random.fold_in(_rk, 511), 0.3 * jnp.ones((16,), jnp.float32), (32, 512))
        _ctx_1024t = jnp.einsum('bsk,bkd->bsd', _ctx_1024c, _ctx_1024P)
        _ctx_1024t = _ctx_1024t * jax.lax.rsqrt(jnp.mean(jnp.square(_ctx_1024t)) + 1e-12) * 0.953939
        ctx_1024 = 2.81802e-05 + 1.00001 * (_ctx_1024t + 0.3 * jax.random.normal(jax.random.fold_in(_rk, 611), (32, 512, 512), jnp.float32))
        itok_SxS2_0_2016 = jax.random.randint(jax.random.fold_in(_rk, 12), (512, 512), 0, 2017, jnp.int32)
        return (x, ctx_1024, itok_SxS2_0_2016)
    x, ctx_1024, itok_SxS2_0_2016 = _rec_inputs()

    def _L0_xattn_setup():
        import jax, jax.numpy as jnp
        import numpy as np
        B, S, DIM, NH = (128, 64, 512, 8)
        DH = DIM // NH
        EPS = 1e-06
        LN_EPS = 1e-05

        def _make_hops(n):
            hops = np.zeros((n, n), dtype=np.int64)
            cur = 1
            for i in range(n):
                for j in range(i + 1, n):
                    hops[i, j] = cur
                    hops[j, i] = cur
                    cur += 1
            return (hops, cur)

        def _mlstm_forward(q, k, v, igate_w, igate_b, fgate_w, fgate_b, rpe, ln_w, ln_b, hops):
            Bq, Sq, _ = q.shape
            pos_emb = rpe[hops]
            gate_in = jnp.concatenate([q, k, v], axis=-1)
            ig = gate_in @ igate_w.T + igate_b
            fg = gate_in @ fgate_w.T + fgate_b
            ig = jnp.transpose(ig, (0, 2, 1))
            fg = jnp.transpose(fg, (0, 2, 1))
            qh = q.reshape(Bq, Sq, NH, DH).transpose(0, 2, 1, 3)
            kh = k.reshape(Bq, Sq, NH, DH).transpose(0, 2, 1, 3)
            vh = v.reshape(Bq, Sq, NH, DH).transpose(0, 2, 1, 3)
            log_f = jax.nn.log_sigmoid(fg)
            csum = jnp.cumsum(log_f, axis=-1)
            csum = jnp.concatenate([jnp.zeros((Bq, NH, 1), csum.dtype), csum], axis=-1)
            lfm = csum[:, :, :, None] - csum[:, :, None, :]
            ltr = jnp.tril(jnp.ones((Sq, Sq), dtype=bool))
            log_fg_matrix = jnp.where(ltr, lfm[:, :, 1:, 1:], -jnp.inf)
            log_D = log_fg_matrix + ig[:, :, None, :]
            max_log_D = jnp.max(log_D, axis=-1, keepdims=True)
            D = jnp.exp(log_D - max_log_D)
            k_scaled = kh / np.sqrt(DH).astype(np.float32)
            pe = pos_emb.reshape(Sq, Sq, NH, DH)
            k_hop = jnp.einsum('bhvc,vmhc->bhvm', qh, pe)
            qk = jnp.einsum('bhsd,bhtd->bhst', qh, k_scaled)
            C = (qk + k_hop) * D
            normalizer = jnp.maximum(jnp.abs(jnp.sum(C, axis=-1, keepdims=True)), jnp.exp(-max_log_D))
            Cn = C / (normalizer + EPS)
            h = Cn @ vh
            mu = jnp.mean(h, axis=-1, keepdims=True)
            var = jnp.mean(jnp.square(h - mu), axis=-1, keepdims=True)
            hn = (h - mu) / jnp.sqrt(var + LN_EPS)
            w = (1.0 + ln_w).reshape(NH, DH)
            b = ln_b.reshape(NH, DH)
            hn = hn * w[None, :, None, :] + b[None, :, None, :]
            return hn.transpose(0, 2, 1, 3).reshape(Bq, Sq, DIM)
        key = jax.random.key(seed)
        ks = jax.random.split(key, 8)
        hops_np, curnum = _make_hops(S)
        return {'q': jax.random.normal(ks[0], (B, S, DIM), dtype=jnp.float32), 'k': jax.random.normal(ks[1], (B, S, DIM), dtype=jnp.float32), 'v': jax.random.normal(ks[2], (B, S, DIM), dtype=jnp.float32), 'igate_w': jax.random.normal(ks[3], (NH, 3 * DIM), dtype=jnp.float32) * 0.02, 'igate_b': jax.random.normal(ks[4], (NH,), dtype=jnp.float32) * 0.1, 'fgate_w': jax.random.normal(ks[5], (NH, 3 * DIM), dtype=jnp.float32) * 0.02, 'fgate_b': jnp.linspace(3.0, 6.0, NH, dtype=jnp.float32), 'rpe': jax.random.normal(ks[6], (curnum, DIM), dtype=jnp.float32) * 0.02, 'ln_w': jax.random.normal(ks[7], (DIM,), dtype=jnp.float32) * 0.1, 'ln_b': jnp.zeros((DIM,), dtype=jnp.float32), 'hops': jnp.asarray(hops_np)}
    _L0_xattn_all = _L0_xattn_setup()
    _L0_xattn_in = {k: v for k, v in _L0_xattn_all.items() if k in ('igate_w', 'igate_b', 'fgate_w', 'fgate_b', 'rpe', 'ln_w', 'ln_b')}
    del _L0_xattn_all

    def _L0_ffn_setup():
        import jax, jax.numpy as jnp
        import numpy as np
        D_MODEL = 512
        D_OUT = 512
        RANK = 16
        NUM_TRUE = 8
        NUM_NULL = 2
        TOP_K = 2
        SCALING = 32.0 / 16.0
        key = jax.random.key(seed)
        ks = jax.random.split(key, 6)
        x = jax.random.normal(ks[0], (4, 2048, D_MODEL), dtype=jnp.float32)
        base_w = jax.random.normal(ks[1], (D_OUT, D_MODEL), dtype=jnp.float32) / np.sqrt(D_MODEL)
        base_b = jax.random.normal(ks[2], (D_OUT,), dtype=jnp.float32) * 0.01
        gate_w = jax.random.normal(ks[3], (NUM_TRUE + NUM_NULL, D_MODEL), dtype=jnp.float32) / np.sqrt(D_MODEL)
        lora_A = jax.random.normal(ks[4], (NUM_TRUE, RANK, D_MODEL), dtype=jnp.float32) / np.sqrt(D_MODEL)
        lora_B = jax.random.normal(ks[5], (NUM_TRUE, D_OUT, RANK), dtype=jnp.float32) * 0.01
        return {'x': x, 'base_w': base_w, 'base_b': base_b, 'gate_w': gate_w, 'lora_A': lora_A, 'lora_B': lora_B}
    _L0_ffn_all = _L0_ffn_setup()
    _L0_ffn_in = {k: v for k, v in _L0_ffn_all.items() if k in ('base_w', 'base_b', 'gate_w', 'lora_A', 'lora_B')}
    del _L0_ffn_all
    return {'x': x, 'ctx_1024': ctx_1024, 'itok_SxS2_0_2016': itok_SxS2_0_2016, 'L0_xattn_igate_w': _L0_xattn_in['igate_w'], 'L0_xattn_igate_b': _L0_xattn_in['igate_b'], 'L0_xattn_fgate_w': _L0_xattn_in['fgate_w'], 'L0_xattn_fgate_b': _L0_xattn_in['fgate_b'], 'L0_xattn_rpe': _L0_xattn_in['rpe'], 'L0_xattn_ln_w': _L0_xattn_in['ln_w'], 'L0_xattn_ln_b': _L0_xattn_in['ln_b'], 'L0_ffn_base_w': _L0_ffn_in['base_w'], 'L0_ffn_base_b': _L0_ffn_in['base_b'], 'L0_ffn_gate_w': _L0_ffn_in['gate_w'], 'L0_ffn_lora_A': _L0_ffn_in['lora_A'], 'L0_ffn_lora_B': _L0_ffn_in['lora_B']}

def reference(x, ctx_1024, itok_SxS2_0_2016, L0_xattn_igate_w, L0_xattn_igate_b, L0_xattn_fgate_w, L0_xattn_fgate_b, L0_xattn_rpe, L0_xattn_ln_w, L0_xattn_ln_b, L0_ffn_base_w, L0_ffn_base_b, L0_ffn_gate_w, L0_ffn_lora_A, L0_ffn_lora_B):
    import jax
    import jax.numpy as jnp

    def _L0_xattn_ref(q, k, v, igate_w, igate_b, fgate_w, fgate_b, rpe, ln_w, ln_b, hops):
        import jax, jax.numpy as jnp
        import numpy as np
        B, S, DIM, NH = (128, 64, 512, 8)
        DH = DIM // NH
        EPS = 1e-06
        LN_EPS = 1e-05

        def _make_hops(n):
            hops = np.zeros((n, n), dtype=np.int64)
            cur = 1
            for i in range(n):
                for j in range(i + 1, n):
                    hops[i, j] = cur
                    hops[j, i] = cur
                    cur += 1
            return (hops, cur)

        def _mlstm_forward(q, k, v, igate_w, igate_b, fgate_w, fgate_b, rpe, ln_w, ln_b, hops):
            Bq, Sq, _ = q.shape
            pos_emb = rpe[hops]
            gate_in = jnp.concatenate([q, k, v], axis=-1)
            ig = gate_in @ igate_w.T + igate_b
            fg = gate_in @ fgate_w.T + fgate_b
            ig = jnp.transpose(ig, (0, 2, 1))
            fg = jnp.transpose(fg, (0, 2, 1))
            qh = q.reshape(Bq, Sq, NH, DH).transpose(0, 2, 1, 3)
            kh = k.reshape(Bq, Sq, NH, DH).transpose(0, 2, 1, 3)
            vh = v.reshape(Bq, Sq, NH, DH).transpose(0, 2, 1, 3)
            log_f = jax.nn.log_sigmoid(fg)
            csum = jnp.cumsum(log_f, axis=-1)
            csum = jnp.concatenate([jnp.zeros((Bq, NH, 1), csum.dtype), csum], axis=-1)
            lfm = csum[:, :, :, None] - csum[:, :, None, :]
            ltr = jnp.tril(jnp.ones((Sq, Sq), dtype=bool))
            log_fg_matrix = jnp.where(ltr, lfm[:, :, 1:, 1:], -jnp.inf)
            log_D = log_fg_matrix + ig[:, :, None, :]
            max_log_D = jnp.max(log_D, axis=-1, keepdims=True)
            D = jnp.exp(log_D - max_log_D)
            k_scaled = kh / np.sqrt(DH).astype(np.float32)
            pe = pos_emb.reshape(Sq, Sq, NH, DH)
            k_hop = jnp.einsum('bhvc,vmhc->bhvm', qh, pe)
            qk = jnp.einsum('bhsd,bhtd->bhst', qh, k_scaled)
            C = (qk + k_hop) * D
            normalizer = jnp.maximum(jnp.abs(jnp.sum(C, axis=-1, keepdims=True)), jnp.exp(-max_log_D))
            Cn = C / (normalizer + EPS)
            h = Cn @ vh
            mu = jnp.mean(h, axis=-1, keepdims=True)
            var = jnp.mean(jnp.square(h - mu), axis=-1, keepdims=True)
            hn = (h - mu) / jnp.sqrt(var + LN_EPS)
            w = (1.0 + ln_w).reshape(NH, DH)
            b = ln_b.reshape(NH, DH)
            hn = hn * w[None, :, None, :] + b[None, :, None, :]
            return hn.transpose(0, 2, 1, 3).reshape(Bq, Sq, DIM)
        return _mlstm_forward(q, k, v, igate_w, igate_b, fgate_w, fgate_b, rpe, ln_w, ln_b, hops)

    def _L0_ffn_ref(x, base_w, base_b, gate_w, lora_A, lora_B):
        import jax, jax.numpy as jnp
        import numpy as np
        D_MODEL = 512
        D_OUT = 512
        RANK = 16
        NUM_TRUE = 8
        NUM_NULL = 2
        TOP_K = 2
        SCALING = 32.0 / 16.0
        xf = x.reshape(-1, x.shape[-1])
        logits = jnp.einsum('td,ed->te', xf, gate_w)
        probs = jax.nn.softmax(logits, axis=-1)
        weights, selected = jax.lax.top_k(probs, TOP_K)
        true_mask = (selected < NUM_TRUE).astype(weights.dtype)
        tw = weights * true_mask
        denom = tw.sum(axis=-1, keepdims=True)
        denom = jnp.where(denom > 0, denom, jnp.ones_like(denom))
        nw = tw / denom
        onehot = jax.nn.one_hot(selected, NUM_TRUE, dtype=nw.dtype)
        ew = jnp.einsum('tk,tke->te', nw, onehot)
        z = jnp.einsum('td,erd->ter', xf, lora_A)
        moe = jnp.einsum('ter,te,eor->to', z, ew, lora_B) * SCALING
        base = jnp.einsum('td,od->to', xf, base_w) + base_b
        out = (base + moe).reshape(x.shape[:-1] + (D_OUT,))
        return out
    x = x + _L0_xattn_ref(_layernorm(x, axis=-1), ctx_1024, ctx_1024, L0_xattn_igate_w, L0_xattn_igate_b, L0_xattn_fgate_w, L0_xattn_fgate_b, L0_xattn_rpe, L0_xattn_ln_w, L0_xattn_ln_b, itok_SxS2_0_2016)
    x = x + _L0_ffn_ref(_layernorm(x, axis=-1), L0_ffn_base_w, L0_ffn_base_b, L0_ffn_gate_w, L0_ffn_lora_A, L0_ffn_lora_B)
    return x

_drawn_inputs = setup_inputs


def setup_inputs(seed=0):
    import zlib

    import numpy as np

    out = dict(_drawn_inputs(seed))
    spreads = {'L0_xattn_ln_b': (0.0, 0.1)}
    factors = {'L0_xattn_igate_b': 64.0, 'L0_ffn_base_b': 8.0}
    for name, (base, spread) in spreads.items():
        noise = np.random.default_rng([zlib.crc32(name.encode()), seed]).standard_normal(out[name].shape)
        drawn = base * np.exp(spread * noise) if base else spread * noise
        out[name] = jnp.asarray(drawn.astype(out[name].dtype))
    for name, factor in factors.items():
        out[name] = (out[name] * factor).astype(out[name].dtype)
    return out
```

```python
from contextlib import ExitStack

import concourse.bass as bass
from concourse import mybir

P = 128
F32 = mybir.dt.float32
I32 = mybir.dt.int32
U32 = mybir.dt.uint32
ALU = mybir.AluOpType
ACT = mybir.ActivationFunctionType
AX_X = mybir.AxisListType.X

BANK = 512
LN_EPS = 1e-5
NORM_EPS = 1e-6
ROUTE_SCALING = 2.0


class Stage:

    BEFORE = 2

    def __init__(self, sem, steps):
        self.sem, self.steps = sem, list(steps)
        self.number = {s: n + 1 for n, s in enumerate(self.steps)}
        self.n = len(self.steps)
        self.at = 0

    def start(self, engine):
        engine.sem_inc(self.sem, self.BEFORE * self.n)

    def step(self, name):
        assert self.steps[self.at % self.n] == name, (name, self.steps[self.at % self.n])
        self.at += 1
        return 1

    def done(self, rnd, name, back=0):
        return rnd * self.n + ((self.BEFORE - back) * self.n + self.number[name])


class Round:

    def __init__(self, k, c):
        self.b, self.par, self.half = k * 2 + c, c % 2, k + c // 2


def build(nc, x, ctxt, hops, igate_w, igate_b, fgate_w, fgate_b, rpe, ln_w, ln_b,
          base_w, base_b, gate_w, lora_A, lora_B, out):
    B, S, DIM = x.shape
    NH = igate_w.shape[0]
    DH = DIM // NH
    KT = DIM // P
    ST = S // P
    E_ALL = gate_w.shape[0]
    E, RANK = lora_A.shape[0], lora_A.shape[1]
    ER = E * RANK
    HPT = P // DH
    assert HPT == 2 and ER == P and B * HPT * 2 == P and ST == 4 and KT == 4
    VG = P // B
    SEG_GROUPS = P // VG
    GROUPS = S // VG
    FG = 32
    GR = FG + NH

    Q_OFF = {3: 0, 0: 512, 2: 640, 1: 1024}
    K_OFF = {0: 0, 1: 512, 3: 896, 2: 1024}
    K_BANKS = [[0], [1, 3], [2]]
    CAUSAL = P * ST * (ST + 1) // 2

    with ExitStack() as ctx:
        def sem(name):
            return ctx.enter_context(nc.semaphore(name))

        psum = ctx.enter_context(nc.psum_tensor("psum", [P, 8 * BANK], F32))
        ARENA = 51900
        arena = ctx.enter_context(nc.sbuf_tensor("arena", [P, ARENA], F32))
        top = [0]

        def place(n):
            top[0] += n
            assert top[0] <= ARENA, top[0]
            return arena[:, top[0] - n:top[0]]

        def bank(n, width=BANK):
            return psum[:, n * BANK:n * BANK + width]

        ident = place(P)
        base_wT = place(KT * DIM).rearrange("p (k o) -> p k o", k=KT)
        route_wT = place(KT * (ER + E_ALL)).rearrange("p (k o) -> p k o", k=KT)
        lora_bT = place(DIM)
        gate_qT = place(KT * GR).rearrange("p (k g) -> p k g", k=KT)
        gate_cT = place(KT * GR).rearrange("p (k g) -> p k g", k=KT)
        ln_w1 = place(DIM)
        ln_b_all = place(DIM)
        base_b_all = place(DIM)
        one = place(1)
        eps_col = place(1)
        experts = place(E_ALL)
        head_mask = place(HPT)
        ig_b = place(1)
        fg_b = place(1)
        after_constants = top[0]

        hopsT = place(ST * S).rearrange("p (t v) -> p t v", t=ST)
        x_group = [place(DIM) for _ in range(2)]
        x_norm = place(DIM)
        x_stats = place(8)
        q_diag = [place(KT * VG * 2 * B) for _ in range(2)]
        index = [place(ST * VG).bitcast(I32) for _ in range(2)]
        rows = [place(ST * DIM).rearrange("p (t d) -> p t d", t=ST) for _ in range(VG)]
        rowsT = [place(KT * S).rearrange("p (k m) -> p k m", k=KT) for _ in range(2)]
        after_hops_small = top[0]
        hop_out = [place(2 * VG * S) for _ in range(2)]
        top[0] = after_hops_small
        hops_raw = place(ST * S)
        base_raw = place(KT * DIM).rearrange("p (t d) -> p t d", t=KT)
        lora_a_raw = place(DIM)
        gate_raw = place(DIM)
        lora_b_raw = place(KT * ER).rearrange("p (t e r) -> p t e r", t=KT, e=E)
        mgate_raw = place(3 * DIM)
        mgate_sum = place(DIM)

        top[0] = after_constants
        xq = [place(DIM) for _ in range(2)]
        xq_norm = place(DIM)
        xq_stats = [place(16) for _ in range(2)]
        ctx_raw = [place(ST * DIM).rearrange("p (t d) -> p t d", t=ST) for _ in range(2)]
        qT = place(KT * S).rearrange("p (k s) -> p k s", k=KT)
        q_padT = place(KT * HPT * S).rearrange("p (k e s) -> p k e s", k=KT, e=HPT)
        kT = [place(KT * S).rearrange("p (k s) -> p k s", k=KT) for _ in range(2)]
        a_all = place(NH * S).rearrange("p (h s) -> p h s", h=NH)
        hop_in = [place(CAUSAL) for _ in range(2)]
        scores = [place(CAUSAL) for _ in range(2)]
        decay = [place(CAUSAL) for _ in range(2)]
        scoresT = [place(CAUSAL) for _ in range(3)]
        attT = place(S)
        att = [place(ST * DIM).rearrange("p (t h d) -> p t h d", t=ST, h=NH) for _ in range(2)]
        x_res = [place(DIM) for _ in range(2)]
        att_c = place(DIM).rearrange("p (h d) -> p h d", h=NH)
        att_sq = place(DIM).rearrange("p (h d) -> p h d", h=NH)
        x1 = [place(DIM) for _ in range(2)]
        x1_b = [place(DIM) for _ in range(2)]
        ffn_x = place(DIM)
        ffn_xT = place(DIM).rearrange("p (k s) -> p k s", k=KT)
        mixT = place(P)
        mix = place(P)
        out_tile = [place(DIM) for _ in range(2)]
        g_z, g_m, g_l, g_c, g_a = [place(S) for _ in range(5)]
        g_rows = place(S)
        statT = [place(ST * GR).rearrange("p (t g) -> p t g", t=ST) for _ in range(2)]
        row_sum = place(ST * NH).rearrange("p (t h) -> p t h", t=ST)
        rden = place(ST * NH).rearrange("p (t h) -> p t h", t=ST)
        head_mu = place(NH)
        head_rs = place(NH)
        f_stats = place(16)
        logits = place(E_ALL)
        probs = place(E_ALL)
        route = place(64)

        hop_dram = [nc.dram_tensor(f"hop_products_{s}", (NH * B, P, P * (s + 1)), F32).ap() for s in range(ST)]
        a_dram = nc.dram_tensor("gate_rows", (B, NH, S), F32).ap()

        weights_loaded = sem("weights_loaded")
        gate_rows_zero = sem("gate_rows_zero")
        mgates_loaded = sem("mgates_loaded")
        pool_setup = sem("pool_setup")
        dve_setup = sem("dve_setup")
        pe_setup = sem("pe_setup")
        passed = {e: sem(f"waits_passed_{e}") for e in ("dve", "pool")}
        setup_evac = sem("setup_evac")

        x_group_loaded = [sem(f"x_group_loaded{i}") for i in range(2)]
        hop_stored = [sem(f"hop_stored{i}") for i in range(2)]
        dve_q = Stage(sem("dve_q"), ["stats", "mean", "norm"])
        pe_q = Stage(sem("pe_q"), ["turn"])
        act_q = Stage(sem("act_q"), ["ln", "rstd", "lo", "hi"])
        gathered = [[sem(f"gathered{s}_{v}") for v in range(VG)] for s in range(ST)]

        def hop_order(nmt):
            tiles = [("turn", v, t) for v in range(VG) for t in range(nmt)]
            order = tiles[:2 * nmt]
            for v in range(VG):
                order.append(("prod", v))
                if v + 2 < VG:
                    order += tiles[(v + 2) * nmt:(v + 3) * nmt]
            return order

        def evacuated_by(nmt, step, part):
            return step[0] == "prod" or (step[1] * nmt + step[2]) % 2 == part

        pe_h, dve_h, act_h, pool_h = [], [], [], []
        for s in range(ST):
            order = hop_order(s + 1)
            pe_h.append(Stage(sem(f"pe_h{s}"), order))
            dve_h.append(Stage(sem(f"dve_h{s}"), [o for o in order if evacuated_by(s + 1, o, 0)]))
            act_h.append(Stage(sem(f"act_h{s}"), [o for o in order if evacuated_by(s + 1, o, 1)]))
            pool_h.append(Stage(sem(f"pool_h{s}"), ["index"]))

        xq_loaded = [sem(f"xq_loaded{i}") for i in range(2)]
        ctx_loaded = [sem(f"ctx_loaded{i}") for i in range(2)]
        a_stored = sem("a_stored")
        a_loaded = [sem(f"a_loaded{h}") for h in range(NH)]
        tiles = range(ST)
        heads = range(NH)
        pairs = range(NH // 2)
        dve_p = Stage(sem("dve_p"), [(n, t) for t in tiles for n in ("stats", "mean", "norm")]
                      + ["z", "abs", "min", "logf", "cum", "a", "cmax", "neg", "maxlog"])
        pe_p = Stage(sem("pe_p"), [("x", t) for t in tiles] + [("c", t) for t in tiles] + ["gates", "stats"])
        act_p = Stage(sem("act_p"), [("ln", 0), ("rstd", 0)]
                      + [s for t in range(1, ST) for s in (("x", t - 1), ("ln", t), ("rstd", t))] + [("x", ST - 1)]
                      + [("c", t) for t in tiles] + ["exp", "ln", "floor", "stats"])
        pool_p = Stage(sem("pool_p"), [("pad", k) for k in range(KT)])
        hop_loaded = [sem(f"hop_loaded{i}") for i in range(2)]
        AHEAD = [[0, 1]] + [[h + 1] for h in range(1, NH - 1)] + [[], []]
        dve_a_steps, pe_a_steps, act_a_steps = [], [], []
        for h in range(NH + 1):
            if h < NH:
                dve_a_steps += [("add", h), ("mul", h)]
                if h % 2:
                    dve_a_steps += [(n, h // 2) for n in ("den", "abs", "eps", "rden")]
                pe_a_steps.append(("qk", h))
            if h == NH:
                pe_a_steps.append(("back", 2))
                dve_a_steps.append(("att", 2))
            if h:
                pe_a_steps += [("turn", h - 1, t) for t in range(3)]
                act_a_steps += [("turn", h - 1, t) for t in range(3)]
            act_a_steps += [("exp", g) for g in AHEAD[h]]
            if h in (3, 5, 7):
                pe_a_steps.append(("pv", (h - 3) // 2))
                act_a_steps.append(("att", (h - 3) // 2))
            if h in (4, 6):
                pe_a_steps.append(("back", (h - 4) // 2))
                dve_a_steps.append(("att", (h - 4) // 2))
            if h == NH:
                pe_a_steps += [("pv", 3), ("back", 3)]
                act_a_steps.append(("att", 3))
                dve_a_steps.append(("att", 3))
        dve_a = Stage(sem("dve_a"), dve_a_steps)
        pe_a = Stage(sem("pe_a"), pe_a_steps)
        act_a = Stage(sem("act_a"), act_a_steps)
        pool_a = Stage(sem("pool_a"), [("mask", h) for h in heads])
        LAYER = [0, 1, 3, 5]
        NORM = [1, 2, 4, 6]
        ROUTE = [2, 3, 5, 7]
        BASE = [3, 4, 6, 8]
        xr_loaded = [sem(f"xr_loaded{i}") for i in range(2)]
        out_stored = [sem(f"out_stored{i}") for i in range(2)]
        dve_f_steps, act_f_steps, pe_f_steps, pool_f_steps = [], [], [], []
        for h in range(NH + 1):
            for t in tiles:
                if ROUTE[t] == h:
                    dve_f_steps.append(("norm", t))
            for t in tiles:
                if LAYER[t] == h:
                    dve_f_steps += [(n, t) for n in ("sum", "mu")]
                    act_f_steps.append(("square", t))
                    pool_f_steps += [(n, t) for n in ("x_b", "center", "scale", "weight")]
            for t in tiles:
                if NORM[t] == h:
                    dve_f_steps += [(n, t) for n in ("x1", "stats", "mean")]
                    pool_f_steps.append(("x1_b", t))
            b_now = [t for t in tiles if BASE[t] == h]
            r_now = [t for t in tiles if ROUTE[t] == h]
            for t in b_now:
                dve_f_steps.append(("out", t))
                act_f_steps.append(("mixT", t))
                pe_f_steps += [("mix", t), ("base", t)]
            dve_f_steps += [("sq_sum", t) for t in tiles if LAYER[t] == h]
            for t in tiles:
                if LAYER[t] == h:
                    act_f_steps += [("head_ln", t), ("head_rs", t)]
            for t in r_now:
                dve_f_steps += [(n, t) for n in ("max", "shift", "rsum", "prob", "top", "where", "which", "first",
                                                 "both", "pick", "guard", "rpick", "weight", "mix")]
                act_f_steps.append(("xT", t))
                pe_f_steps += [("turn", t), ("route", t)]
            for t in tiles:
                if NORM[t] == h:
                    act_f_steps += [("ln", t), ("rstd", t)]
            act_f_steps += [("exp", t) for t in r_now]
        dve_f = Stage(sem("dve_f"), dve_f_steps)
        act_f = Stage(sem("act_f"), act_f_steps)
        pe_f = Stage(sem("pe_f"), pe_f_steps)
        pool_f = Stage(sem("pool_f"), pool_f_steps)

        passed_total = dict.fromkeys(passed, 0)
        repeats = [1]

        def stand_alone(engine, name):
            engine.sem_inc(passed[name], 1)
            passed_total[name] += repeats[0]

        def all_passed(engine, name):
            engine.wait_ge(passed[name], passed_total[name])

        x_groups = x.rearrange("b (g v) d -> g v b d", v=VG)
        x_tiles = x.rearrange("b (t p) d -> b t p d", p=P)
        out_tiles = out.rearrange("b (t p) d -> b t p d", p=P)
        ctx_tiles = ctxt.rearrange("b (t p) d -> b p t d", p=P)
        hop_store = [d.rearrange("(i p) (g v) m -> i g p (v m)", p=P, v=VG) for d in hop_dram]
        hop_load = [d.rearrange("(h b) v m -> h b v m", b=B) for d in hop_dram]

        base_o = base_w.rearrange("(t p) d -> p t d", p=P)
        hops_f = rows[0]
        jobs = []
        for t in range(ST):
            jobs.append(([hops_f[:, u, t * P:(t + 1) * P] for u in range(ST)], P, P,
                         hopsT[:, t, :].bitcast(I32), 1.0, False))
        for k in range(KT):
            jobs.append(([base_raw[:, t, k * P:(k + 1) * P] for t in range(KT)], P, P, base_wT[:, k, :], 1.0, False))
        jobs.append(([lora_a_raw[:, k * P:(k + 1) * P] for k in range(KT)], P, ER, route_wT[:, :, 0:ER], 1.0, True))
        jobs.append(([gate_raw[0:E_ALL, k * P:(k + 1) * P] for k in range(KT)], E_ALL, E_ALL,
                     route_wT[:, :, ER:ER + E_ALL], 1.0, True))
        jobs.append(([lora_b_raw[:, t, :, :].rearrange("p e r -> p (e r)") for t in range(KT)], P, P,
                     lora_bT, ROUTE_SCALING, False))
        jobs.append(([mgate_raw[0:GR, k * P:(k + 1) * P] for k in range(KT)], GR, GR, gate_qT, 1.0, True))
        K_SCALE = float(DH) ** -0.5
        jobs.append(([mgate_sum[0:GR, k * P:(k + 1) * P] for k in range(KT)], GR, GR, gate_cT, 1.0 / K_SCALE, True))
        N_WEIGHTS = 16 * 10

        block = ctx.enter_context(nc.Block())

        def segment_over(engine, s):
            if s:
                for stages in (pe_h, dve_h, act_h, pool_h):
                    last = stages[s - 1]
                    engine.wait_ge(last.sem, last.done(SEG_GROUPS - 1, last.steps[-1]))

        def hops_over(engine):
            segment_over(engine, ST)
            for i in range(2):
                engine.wait_ge(hop_stored[i], 32 * (GROUPS // 2 + 1))
            engine.wait_ge(dve_q.sem, dve_q.done(GROUPS - 1, "norm"))
            engine.wait_ge(pe_q.sem, pe_q.done(GROUPS - 1, "turn"))
            engine.wait_ge(act_q.sem, act_q.done(GROUPS - 1, "hi"))

        def hop_segments(engine, body):
            for s in range(ST):
                segment_over(engine, s)
                pairs_here = SEG_GROUPS // 2
                last = s == ST - 1
                repeats[0] = pairs_here - 1 if last else pairs_here
                with engine.Fori(0, repeats[0]) as k:
                    body(s, k, False)
                repeats[0] = 1
                if last:
                    body(s, pairs_here - 1, True)

        def rounds(run):
            def body(k, c, which):
                run(Round(k, c + 1) if "p" in which else None, Round(k, c) if "a" in which else None,
                    Round(k, c - 1) if "f" in which else None)
            return body

        def batch_loop(engine, run):
            body = rounds(run)
            body(0, -1, "p")
            body(0, 0, "pa")
            repeats[0] = B // 2 - 1
            with engine.Fori(0, repeats[0]) as k:
                body(k, 1, "paf")
                body(k, 2, "paf")
            repeats[0] = 1
            body(0, B - 1, "af")
            body(0, B, "f")

        def hop_copy(engine, copy, stages, s, g, k, par, o, part):
            nmt = s + 1
            stage = stages[s]
            engine.wait_ge(pe_h[s].sem, pe_h[s].done(g, o))
            v = o[1]
            if o[0] == "turn":
                n = v * nmt + o[2]
                engine.wait_ge(pe_h[s].sem, pe_h[s].done(g, ("prod", (v - 2) % VG), 1 if v < 2 else 0))
                copy(rowsT[v % 2][:, :, o[2] * P:(o[2] + 1) * P],
                     bank(1 + n % 2).rearrange("p (k m) -> p k m", k=KT)).then_inc(stage.sem, stage.step(o))
            else:
                if v == 0:
                    engine.wait_ge(hop_stored[par], k * 32 + (SEG_GROUPS // 2 * s + 1) * 32)
                i = 1 - part
                width = P * nmt
                lo = (i * VG + v) * width
                copy(hop_out[par][:, lo:lo + width], bank(3 + 2 * (v % 2) + i, width)).then_inc(
                    stage.sem, stage.step(o))

        @block.sync
        def _(sp):
            for i in range(2):
                sp.sem_inc(hop_stored[i], 32)
                sp.sem_inc(out_stored[i], 32)
            sp.dma_start(hops_raw.bitcast(I32).rearrange("p (t m) -> p t m", t=ST),
                         hops.rearrange("(t p) m -> p t m", p=P)).then_inc(weights_loaded, 16)
            sp.dma_start(base_raw, base_o).then_inc(weights_loaded, 16)
            sp.dma_start(lora_a_raw, lora_A.rearrange("e r d -> (e r) d")).then_inc(weights_loaded, 16)
            sp.dma_start(gate_raw[0:E_ALL, :], gate_w[:, :]).then_inc(weights_loaded, 16)
            for t in range(KT):
                sp.dma_start(lora_b_raw[:, t, :, :],
                             lora_B.rearrange("e (t o) r -> t o e r", t=KT)[t]).then_inc(weights_loaded, 16)
            sp.dma_start(ln_w1, ln_w.partition_broadcast(P)).then_inc(weights_loaded, 16)
            sp.dma_start(ln_b_all, ln_b.partition_broadcast(P)).then_inc(weights_loaded, 16)
            sp.wait_ge(gate_rows_zero, 1)
            for dst, src in ((mgate_raw[0:NH, :], igate_w[:, :]), (mgate_raw[FG:GR, :], fgate_w[:, :]),
                             (ig_b[0:NH, :], igate_b.rearrange("(h o) -> h o", o=1)),
                             (fg_b[FG:GR, :], fgate_b.rearrange("(h o) -> h o", o=1)),
                             (base_b_all, base_b.partition_broadcast(P))):
                sp.dma_start(dst, src).then_inc(mgates_loaded, 16)

            def load_group(par, g):
                for v in range(VG):
                    sp.dma_start(x_group[par][v * B:(v + 1) * B, :], x_groups[g, v, :, :]).then_inc(
                        x_group_loaded[par], 16)

            load_group(0, 0)
            load_group(1, 1)
            sp.wait_ge(setup_evac, len(jobs))

            def hop_body(s, k, last):
                width = VG * P * (s + 1)
                for par in range(2):
                    g = k * 2 + par
                    if not last:
                        gg = g + SEG_GROUPS * s
                        sp.wait_ge(dve_q.sem, dve_q.done(gg, "norm"))
                        load_group(par, gg + 2)
                    sp.wait_ge(dve_h[s].sem, dve_h[s].done(g, ("prod", VG - 1)))
                    sp.wait_ge(act_h[s].sem, act_h[s].done(g, ("prod", VG - 1)))
                    for i in range(2):
                        sp.dma_start(hop_store[s][i, g, :, :],
                                     hop_out[par][:, i * width:(i + 1) * width]).then_inc(hop_stored[par], 16)

            hop_segments(sp, hop_body)
            hops_over(sp)

            def load_xq(r, t):
                sp.wait_ge(dve_p.sem, dve_p.done(r.b, ("norm", (t - 2) % ST), 1 if t < 2 else 0))
                sp.dma_start(xq[t % 2], x_tiles[r.b, t, :, :]).then_inc(xq_loaded[t % 2], 16)

            def load_hop(r, h):
                sp.wait_ge(dve_a.sem, dve_a.done(r.b, ("add", (h - 2) % NH), 1 if h < 2 else 0))
                for i in range(ST):
                    sp.dma_start(hop_in[h % 2][:, Q_OFF[i]:Q_OFF[i] + P * (i + 1)],
                                 hop_load[i][h, r.b, :, :]).then_inc(hop_loaded[h % 2], 16)

            def load_a(r, h):
                sp.wait_ge(act_a.sem, act_a.done(r.b, ("exp", h), 1))
                if h == 0:
                    sp.wait_ge(a_stored, r.b * 16 + 16)
                sp.dma_start(a_all[:, h, :], a_dram[r.b, h, :].partition_broadcast(P)).then_inc(a_loaded[h], 16)

            def run(rp, ra, rf):
                if rp:
                    sp.wait_ge(pe_a.sem, pe_a.done(rp.b, ("pv", 3), 2))
                    sp.dma_start(ctx_raw[rp.par], ctx_tiles[rp.b, :, :, :]).then_inc(ctx_loaded[rp.par], 16)
                for h in range(NH + 1):
                    if ra and h < NH - 1:
                        load_hop(ra, h + 1)
                    if rp and h == NH - 1:
                        load_hop(rp, 0)
                    if rp and h < ST:
                        load_xq(rp, h)
                    if rp and h == 6:
                        sp.wait_ge(dve_p.sem, dve_p.done(rp.b, "a"))
                        sp.dma_start(a_dram[rp.b, :, :], g_a[0:NH, :]).then_inc(a_stored, 16)
                    if rp and h == 7:
                        for i in range(NH - 1):
                            load_a(rp, i)
                    if rp and h == 8:
                        load_a(rp, NH - 1)
                    for t in tiles:
                        if rf and LAYER[t] == h:
                            sp.wait_ge(dve_f.sem, dve_f.done(rf.b, ("x1", (t - 2) % ST), 1 if t < 2 else 0))
                            sp.dma_start(x_res[t % 2], x_tiles[rf.b, t, :, :]).then_inc(xr_loaded[t % 2], 16)
                    for t in tiles:
                        if rf and BASE[t] == h:
                            sp.wait_ge(dve_f.sem, dve_f.done(rf.b, ("out", t)))
                            sp.dma_start(out_tiles[rf.b, t, :, :], out_tile[t % 2]).then_inc(out_stored[t % 2], 16)

            batch_loop(sp, run)
            for i in range(2):
                sp.wait_ge(out_stored[i], 16 * (2 * B) + 32)

        @block.gpsimd
        def _(pool):
            for s in range(ST):
                pool_h[s].start(pool)
            for st in (pool_p, pool_a, pool_f):
                st.start(pool)
            nc.gpsimd.memset(ident, 0.0).then_inc(pool_setup, 1)
            pool.wait_ge(pool_setup, 1)
            nc.gpsimd.affine_select(out=ident, in_=ident, compare_op=ALU.not_equal, fill=1.0, base=0,
                                    pattern=[[-1, P]], channel_multiplier=1).then_inc(pool_setup, 1)
            nc.gpsimd.memset(head_mask, 1.0).then_inc(pool_setup, 1)
            pool.wait_ge(pool_setup, 3)
            nc.gpsimd.affine_select(out=head_mask[:, 0:1], in_=head_mask[:, 0:1], compare_op=ALU.is_ge, fill=0.0,
                                    base=DH - 1, pattern=[[0, 1]], channel_multiplier=-1)
            nc.gpsimd.affine_select(out=head_mask[:, 1:2], in_=head_mask[:, 1:2], compare_op=ALU.is_ge, fill=0.0,
                                    base=-DH, pattern=[[0, 1]], channel_multiplier=1).then_inc(pool_setup, 1)
            nc.gpsimd.iota(experts.bitcast(I32), pattern=[[1, E_ALL]], base=0,
                           channel_multiplier=0).then_inc(pool_setup, 1)
            pool.wait_ge(pool_setup, 5)
            pool.wait_ge(setup_evac, len(jobs))

            def hop_body(s, k, last):
                nmt = s + 1
                for par in range(2):
                    g = k * 2 + par
                    here = index[par][:, 0:nmt * VG].rearrange("p (t v) -> p t v", t=nmt)
                    groups = hopsT.bitcast(I32).rearrange("p t (g v) -> p g t v", v=VG)
                    pool.wait_ge(pe_h[s].sem, pe_h[s].done(g, ("turn", VG - 1, nmt - 1), 2))
                    stand_alone(pool, "pool")
                    nc.gpsimd.tensor_copy(here, groups[:, g + SEG_GROUPS * s, 0:nmt, :]).then_inc(
                        pool_h[s].sem, pool_h[s].step("index"))
                    pool.wait_ge(pool_h[s].sem, pool_h[s].done(g, "index"))
                    for v in range(VG):
                        pool.wait_ge(pe_h[s].sem, pe_h[s].done(g, ("turn", v, nmt - 1), 1))
                        stand_alone(pool, "pool")
                        for t in range(nmt):
                            nc.gpsimd.indirect_dma_start(
                                out=rows[v][:, t, :], out_offset=None, in_=rpe[:, :],
                                in_offset=bass.IndirectOffsetOnAxis(ap=here[:, t, v:v + 1].bitcast(U32), axis=0),
                            ).then_inc(gathered[s][v], 16)

            hop_segments(pool, hop_body)
            hops_over(pool)

            def run(rp, ra, rf):
                def mask_future(h):
                    pool.wait_ge(act_a.sem, act_a.done(ra.b, ("exp", h)))
                    d = decay[h % 2]
                    stand_alone(pool, "pool")
                    for part in (d[:, 3 * P:5 * P].rearrange("p (a s) -> p a s", a=2),
                                 d[:, 6 * P:10 * P].rearrange("p (a s) -> p a s", a=2)[:, :, P:2 * P]):
                        last = nc.gpsimd.affine_select(out=part, in_=part, compare_op=ALU.is_ge, fill=0.0, base=0,
                                                       pattern=[[0, 2], [-1, P]], channel_multiplier=1)
                    last.then_inc(pool_a.sem, pool_a.step(("mask", h)))

                for h in range(NH + 1):
                    if ra:
                        for g in AHEAD[h]:
                            mask_future(g)
                    for t in tiles:
                        if rf and LAYER[t] == h:
                            pool.wait_ge(xr_loaded[t % 2], rf.b * 32 + 16 * (t // 2 + 1))
                            nc.gpsimd.tensor_tensor(x_res[t % 2], x_res[t % 2], ln_b_all, ALU.add).then_inc(
                                pool_f.sem, pool_f.step(("x_b", t)))
                            pool.wait_ge(dve_f.sem, dve_f.done(rf.b, ("mu", t)))
                            pool.wait_ge(dve_f.sem, dve_f.done(rf.b, ("x1", (t - 1) % ST), 1 if t < 1 else 0))
                            nc.gpsimd.tensor_tensor(att_c, att[rf.par][:, t, :, :],
                                                    head_mu.unsqueeze(2).to_broadcast([P, NH, DH]), ALU.add).then_inc(
                                pool_f.sem, pool_f.step(("center", t)))
                            pool.wait_ge(act_f.sem, act_f.done(rf.b, ("head_rs", t)))
                            nc.gpsimd.tensor_tensor(att_c, att_c, head_rs.unsqueeze(2).to_broadcast([P, NH, DH]),
                                                    ALU.mult).then_inc(pool_f.sem, pool_f.step(("scale", t)))
                            pool.wait_ge(pool_f.sem, pool_f.done(rf.b, ("scale", t)))
                            flat = att_c.rearrange("p h d -> p (h d)")
                            nc.gpsimd.tensor_tensor(flat, flat, ln_w1, ALU.mult).then_inc(
                                pool_f.sem, pool_f.step(("weight", t)))
                    for t in tiles:
                        if rf and NORM[t] == h:
                            pool.wait_ge(dve_f.sem, dve_f.done(rf.b, ("x1", t)))
                            pool.wait_ge(dve_f.sem, dve_f.done(rf.b, ("out", (t - 2) % ST), 1 if t < 2 else 0))
                            nc.gpsimd.tensor_tensor(x1_b[t % 2], x1[t % 2], base_b_all, ALU.add).then_inc(
                                pool_f.sem, pool_f.step(("x1_b", t)))
                    for k, at in enumerate((5, 6, 7, 8)):
                        if rp and h == at:
                            pool.wait_ge(pe_a.sem, pe_a.done(rp.b, ("qk", 2 * k + 1), 1))
                            pool.wait_ge(act_p.sem, act_p.done(rp.b, ("x", ST - 1)))
                            stand_alone(pool, "pool")
                            for e in range(HPT):
                                last = nc.gpsimd.tensor_scalar(q_padT[:, k, e, :], qT[:, k, :], head_mask[:, e:e + 1],
                                                               None, ALU.mult)
                            last.then_inc(pool_p.sem, pool_p.step(("pad", k)))

            batch_loop(pool, run)
            all_passed(pool, "pool")

        @block.scalar
        def _(act):
            def rstd(stage, rnd, ln, power, dst, variance, scale=1.0):
                nc.scalar.activation(dst, variance, ACT.Ln, bias=eps_col, scale=scale).then_inc(
                    stage.sem, stage.step(ln))
                act.wait_ge(stage.sem, stage.done(rnd, ln))
                nc.scalar.activation(dst, dst, ACT.Exp, scale=-0.5).then_inc(stage.sem, stage.step(power))

            nc.scalar.preload_act_table_set("natural_log_exp_and_others")
            act_q.start(act)
            for s in range(ST):
                act_h[s].start(act)
            for st in (act_p, act_a, act_f):
                st.start(act)
            act.wait_ge(setup_evac, len(jobs))

            def queries(par, g):
                stats(g)
                turned(par, g)

            def stats(g):
                act.wait_ge(dve_q.sem, dve_q.done(g, "mean"))
                rstd(act_q, g, "ln", "rstd", x_stats[:, 7:8], x_stats[:, 7:8])

            def turned(par, g):
                act.wait_ge(pe_q.sem, pe_q.done(g, "turn"))
                src = bank(0).rearrange("p (k b) -> p k b", b=B)
                dst = q_diag[par].rearrange("p (k e b) -> p k e b", e=2, b=B)
                for e, name in enumerate(("lo", "hi")):
                    rows_e = slice(e * DH, (e + 1) * DH)
                    nc.scalar.copy(dst[rows_e, :, e, :], src[rows_e]).then_inc(act_q.sem, act_q.step(name))

            act.wait_ge(dve_setup, 4)
            queries(0, 0)

            def hop_body(s, k, last):
                nmt = s + 1
                for par in range(2):
                    g = k * 2 + par
                    for o in hop_order(nmt):
                        ahead = g + (SEG_GROUPS * s + 1)
                        if o == ("prod", 1) and not (last and par):
                            stats(ahead)
                        if o == ("prod", VG - 2) and not (last and par):
                            act.wait_ge(pe_h[s].sem, pe_h[s].done(g, ("prod", VG - 1), 1))
                            turned(1 - par, ahead)
                        if evacuated_by(nmt, o, 1):
                            hop_copy(act, nc.scalar.copy, act_h, s, g, k, par, o, 1)

            hop_segments(act, hop_body)
            hops_over(act)

            def run(rp, ra, rf):
                def prepared(t, what):
                    act.wait_ge(pe_p.sem, pe_p.done(rp.b, (what, t)))
                    src = bank(6).rearrange("p (k s) -> p k s", k=KT)
                    if what == "x":
                        if t == 0:
                            act.wait_ge(pool_p.sem, pool_p.done(rp.b, ("pad", KT - 1), 1))
                            act.wait_ge(pe_p.sem, pe_p.done(rp.b, "gates", 1))
                        nc.scalar.copy(qT[:, :, t * P:(t + 1) * P], src).then_inc(act_p.sem, act_p.step(("x", t)))
                    else:
                        if t == 0:
                            act.wait_ge(pe_a.sem, pe_a.done(rp.b, ("qk", NH - 1), 2))
                        nc.scalar.mul(kT[rp.par][:, :, t * P:(t + 1) * P], src, K_SCALE).then_inc(
                            act_p.sem, act_p.step(("c", t)))

                def gates():
                    act.wait_ge(dve_p.sem, dve_p.done(rp.b, "abs"))
                    nc.scalar.activation(g_l[0:NH, :], g_l[0:NH, :], ACT.Exp, scale=-1.0).then_inc(
                        act_p.sem, act_p.step("exp"))
                    act.wait_ge(act_p.sem, act_p.done(rp.b, "exp"))
                    nc.scalar.activation(g_l[0:NH, :], g_l[0:NH, :], ACT.Ln, bias=1.0).then_inc(
                        act_p.sem, act_p.step("ln"))

                def floors():
                    act.wait_ge(dve_p.sem, dve_p.done(rp.b, "maxlog"))
                    nc.scalar.activation(g_rows[FG:GR, :], g_c[0:NH, :], ACT.Exp, scale=-1.0).then_inc(
                        act_p.sem, act_p.step("floor"))

                def head_decay(h):
                    act.wait_ge(a_loaded[h], ra.b * 16 + 16)
                    if h == 0:
                        act.wait_ge(act_p.sem, act_p.done(ra.b, "stats"))
                    act.wait_ge(dve_a.sem, dve_a.done(ra.b, ("mul", (h - 2) % NH), 1 if h < 2 else 0))
                    for i in range(ST):
                        last = nc.scalar.activation(decay[h % 2][:, Q_OFF[i]:Q_OFF[i] + P * (i + 1)],
                                                    a_all[:, h, 0:P * (i + 1)], ACT.Exp,
                                                    bias=statT[ra.par][:, i, h:h + 1])
                    last.then_inc(act_a.sem, act_a.step(("exp", h)))

                for h in range(NH + 1):
                    if ra and h:
                        g = h - 1
                        for n, group in enumerate(K_BANKS):
                            act.wait_ge(pe_a.sem, pe_a.done(ra.b, ("turn", g, n)))
                            if n == 0:
                                before = (g - 3) // 2 if g >= 3 else NH // 2 - 1
                                act.wait_ge(pe_a.sem, pe_a.done(ra.b, ("pv", before), 1 if g < 3 else 0))
                            lo = K_OFF[group[0]]
                            width = sum(P * (ST - j) for j in group)
                            nc.scalar.copy(scoresT[g % 3][:, lo:lo + width],
                                           bank(3 + (3 * g + n) % 2, width)).then_inc(
                                act_a.sem, act_a.step(("turn", g, n)))
                    if ra:
                        for g in AHEAD[h]:
                            head_decay(g)
                    if rp and h == 7:
                        floors()
                        act.wait_ge(pe_p.sem, pe_p.done(rp.b, "stats"))
                        act.wait_ge(act_a.sem, act_a.done(rp.b, ("exp", NH - 1), 2))
                        act.wait_ge(dve_a.sem, dve_a.done(rp.b, ("den", NH // 2 - 1), 2))
                        nc.scalar.copy(statT[rp.par], bank(6).rearrange("p (t s) -> p t s", t=ST)[:, :, 0:GR]).then_inc(act_p.sem, act_p.step("stats"))
                    for t in tiles:
                        if rf and LAYER[t] == h:
                            act.wait_ge(pool_f.sem, pool_f.done(rf.b, ("center", t)))
                            act.wait_ge(dve_f.sem, dve_f.done(rf.b, ("sq_sum", (t - 1) % ST), 1 if t < 1 else 0))
                            nc.scalar.square(att_sq, att_c).then_inc(act_f.sem, act_f.step(("square", t)))
                    for t in tiles:
                        if rf and BASE[t] == h:
                            act.wait_ge(pe_f.sem, pe_f.done(rf.b, ("mix", t)))
                            act.wait_ge(pe_f.sem, pe_f.done(rf.b, ("base", (t - 1) % ST), 1 if t < 1 else 0))
                            nc.scalar.copy(mixT, bank(7, P)).then_inc(act_f.sem, act_f.step(("mixT", t)))
                    for t in tiles:
                        if rf and LAYER[t] == h:
                            act.wait_ge(dve_f.sem, dve_f.done(rf.b, ("sq_sum", t)))
                            rstd(act_f, rf.b, ("head_ln", t), ("head_rs", t), head_rs, head_rs, 1.0 / DH)
                    for t in tiles:
                        if rf and ROUTE[t] == h:
                            act.wait_ge(pe_f.sem, pe_f.done(rf.b, ("turn", t)))
                            act.wait_ge(pe_f.sem, pe_f.done(rf.b, ("base", (t - 1) % ST), 1 if t < 1 else 0))
                            nc.scalar.copy(ffn_xT.rearrange("p k s -> p (k s)"), bank(7)).then_inc(
                                act_f.sem, act_f.step(("xT", t)))
                    if rp and 1 <= h <= ST:
                        prepared(h - 1, "x")
                    if rp and h == 4:
                        prepared(0, "c")
                        prepared(1, "c")
                    if rp and h == 5:
                        prepared(2, "c")
                        prepared(3, "c")
                    if ra:
                        p = {3: 0, 5: 1, 7: 2, 8: 3}.get(h)
                        if p is not None:
                            act.wait_ge(pe_a.sem, pe_a.done(ra.b, ("pv", p)))
                            nc.scalar.copy(attT, bank(5)).then_inc(act_a.sem, act_a.step(("att", p)))
                    for t in tiles:
                        if rf and NORM[t] == h:
                            act.wait_ge(dve_f.sem, dve_f.done(rf.b, ("mean", t)))
                            rstd(act_f, rf.b, ("ln", t), ("rstd", t), f_stats[:, 7:8], f_stats[:, 7:8])
                    if rp and h < ST:
                        act.wait_ge(dve_p.sem, dve_p.done(rp.b, ("mean", h)))
                        st = xq_stats[h % 2]
                        rstd(act_p, rp.b, ("ln", h), ("rstd", h), st[:, 7:8], st[:, 7:8])
                    for t in tiles:
                        if rf and ROUTE[t] == h:
                            act.wait_ge(dve_f.sem, dve_f.done(rf.b, ("shift", t)))
                            nc.scalar.activation(probs, logits, ACT.Exp, accum_out=route[:, 1:2]).then_inc(
                                act_f.sem, act_f.step(("exp", t)))
                    if rp and h == 5:
                        gates()

            batch_loop(act, run)

        @block.vector
        def _(dve):
            dve_q.start(dve)
            for s in range(ST):
                dve_h[s].start(dve)
            for st in (dve_p, dve_a, dve_f):
                st.start(dve)
            nc.vector.memset(mgate_raw, 0.0).then_inc(gate_rows_zero, 1)
            nc.vector.memset(one, 1.0).then_inc(dve_setup, 1)
            nc.vector.memset(eps_col, LN_EPS).then_inc(dve_setup, 1)
            for i in range(2):
                nc.vector.memset(q_diag[i], 0.0).then_inc(dve_setup, 1)
            dve.wait_ge(weights_loaded, N_WEIGHTS)
            dve.wait_ge(mgates_loaded, 16 * 5)
            dve.wait_ge(pool_setup, 5)
            nc.vector.tensor_copy(hops_f, hops_raw.bitcast(I32).rearrange("p (t m) -> p t m", t=ST)).then_inc(
                dve_setup, 1)
            nc.vector.tensor_tensor(mgate_sum[0:GR, :], mgate_raw[0:GR, DIM:2 * DIM], mgate_raw[0:GR, 2 * DIM:3 * DIM],
                                    ALU.add).then_inc(dve_setup, 1)
            nc.vector.tensor_scalar(ln_w1, ln_w1, 1.0, None, ALU.add).then_inc(dve_setup, 1)
            nc.vector.tensor_copy(experts, experts.bitcast(I32)).then_inc(dve_setup, 1)
            for n, (srcs, rows_in, cols, dst, scale, split) in enumerate(jobs):
                dve.wait_ge(pe_setup, n + 1)
                src = bank(n % 8, len(srcs) * cols)
                if split:
                    src = src.rearrange("p (k c) -> p k c", k=len(srcs))
                nc.vector.tensor_scalar(dst, src, scale, None, ALU.mult).then_inc(setup_evac, 1)
            dve.wait_ge(setup_evac, len(jobs))

            def query_stats(par, g, half):
                dve.wait_ge(x_group_loaded[par], half * 64 + 64)
                nc.vector.bn_stats(x_stats[:, 0:6], x_group[par]).then_inc(dve_q.sem, dve_q.step("stats"))
                dve.wait_ge(dve_q.sem, dve_q.done(g, "stats"))
                stand_alone(dve, "dve")
                nc.vector.bn_aggr(x_stats[:, 6:8], x_stats[:, 0:6]).then_inc(dve_q.sem, dve_q.step("mean"))

            def query_norm(par, g):
                dve.wait_ge(act_q.sem, act_q.done(g, "rstd"))
                dve.wait_ge(pe_q.sem, pe_q.done(g, "turn", 1))
                nc.vector.tensor_scalar(x_norm, x_group[par], x_stats[:, 6:7], x_stats[:, 7:8], ALU.subtract,
                                        ALU.mult).then_inc(dve_q.sem, dve_q.step("norm"))

            query_stats(0, 0, 0)
            query_norm(0, 0)

            def hop_body(s, k, last):
                nmt = s + 1
                for par in range(2):
                    g = k * 2 + par
                    ahead = g + (SEG_GROUPS * s + 1)
                    for o in hop_order(nmt):
                        if evacuated_by(nmt, o, 0):
                            hop_copy(dve, nc.vector.tensor_copy, dve_h, s, g, k, par, o, 0)
                        if o == ("prod", 0) and not (last and par):
                            query_stats(1 - par, ahead, k + (SEG_GROUPS // 2 * s + par))
                        if o == ("prod", 1) and not (last and par):
                            query_norm(1 - par, ahead)

            hop_segments(dve, hop_body)
            hops_over(dve)
            nc.vector.memset(g_rows, 0.0).then_inc(dve_setup, 1)
            dve.wait_ge(dve_setup, 9)

            def run(rp, ra, rf):
                def stats_query(t):
                    st = xq_stats[t % 2]
                    dve.wait_ge(xq_loaded[t % 2], rp.b * 32 + 16 * (t // 2 + 1))
                    nc.vector.bn_stats(st[:, 0:6], xq[t % 2]).then_inc(dve_p.sem, dve_p.step(("stats", t)))
                    dve.wait_ge(dve_p.sem, dve_p.done(rp.b, ("stats", t)))
                    stand_alone(dve, "dve")
                    nc.vector.bn_aggr(st[:, 6:8], st[:, 0:6]).then_inc(dve_p.sem, dve_p.step(("mean", t)))

                def norm_query(t):
                    st = xq_stats[t % 2]
                    dve.wait_ge(act_p.sem, act_p.done(rp.b, ("rstd", t)))
                    dve.wait_ge(pe_p.sem, pe_p.done(rp.b, ("x", (t - 1) % ST), 1 if t < 1 else 0))
                    nc.vector.tensor_scalar(xq_norm, xq[t % 2], st[:, 6:7], st[:, 7:8], ALU.subtract,
                                            ALU.mult).then_inc(dve_p.sem, dve_p.step(("norm", t)))

                def gates_1():
                    dve.wait_ge(pe_p.sem, pe_p.done(rp.b, "gates"))
                    G = bank(6)
                    nc.vector.tensor_scalar(g_z[0:NH, :], G[FG:GR, :], fg_b[FG:GR, :], None, ALU.add).then_inc(
                        dve_p.sem, dve_p.step("z"))
                    dve.wait_ge(dve_p.sem, dve_p.done(rp.b, "z"))
                    nc.vector.scalar_tensor_tensor(g_l[0:NH, :], g_z[0:NH, :], -1.0, g_z[0:NH, :], ALU.mult,
                                                   ALU.max).then_inc(
                        dve_p.sem, dve_p.step("abs"))
                    nc.vector.tensor_scalar(g_m[0:NH, :], g_z[0:NH, :], 0.0, None, ALU.min).then_inc(
                        dve_p.sem, dve_p.step("min"))

                def gates_2():
                    G = bank(6)
                    dve.wait_ge(act_p.sem, act_p.done(rp.b, "ln"))
                    dve.wait_ge(dve_p.sem, dve_p.done(rp.b, "min"))
                    nc.vector.tensor_tensor(g_m[0:NH, :], g_m[0:NH, :], g_l[0:NH, :], ALU.subtract).then_inc(
                        dve_p.sem, dve_p.step("logf"))
                    dve.wait_ge(dve_p.sem, dve_p.done(rp.b, "logf"))
                    dve.wait_ge(act_p.sem, act_p.done(rp.b, "floor", 1))
                    nc.vector.tensor_tensor_scan(g_c[0:NH, :], one[0:NH, :].to_broadcast([NH, S]), g_m[0:NH, :], 0.0, ALU.mult,
                                                 ALU.add).then_inc(dve_p.sem, dve_p.step("cum"))
                    dve.wait_ge(dve_p.sem, dve_p.done(rp.b, "cum"))
                    if not isinstance(rp.b, int) or rp.b:
                        dve.wait_ge(a_stored, rp.b * 16)
                    nc.vector.scalar_tensor_tensor(g_a[0:NH, :], G[0:NH, :], ig_b[0:NH, :], g_c[0:NH, :], ALU.add,
                                                   ALU.subtract).then_inc(dve_p.sem, dve_p.step("a"))
                    dve.wait_ge(dve_p.sem, dve_p.done(rp.b, "a"))
                    nc.vector.tensor_tensor_scan(g_z[0:NH, :], g_a[0:NH, :], g_a[0:NH, :], -3.0e38, ALU.max,
                                                 ALU.max).then_inc(dve_p.sem, dve_p.step("cmax"))
                    dve.wait_ge(dve_p.sem, dve_p.done(rp.b, "cmax"))
                    dve.wait_ge(pe_p.sem, pe_p.done(rp.b, "stats", 1))
                    nc.vector.tensor_scalar(g_rows[0:NH, :], g_z[0:NH, :], -1.0, None, ALU.mult).then_inc(
                        dve_p.sem, dve_p.step("neg"))
                    nc.vector.tensor_tensor(g_c[0:NH, :], g_c[0:NH, :], g_z[0:NH, :], ALU.add).then_inc(
                        dve_p.sem, dve_p.step("maxlog"))

                def head_out(p):
                    dve.wait_ge(pe_a.sem, pe_a.done(ra.b, ("back", p)))
                    dve.wait_ge(dve_a.sem, dve_a.done(ra.b, ("rden", p)))
                    dve.wait_ge(pool_f.sem, pool_f.done(ra.b, ("center", ST - 1), 2))
                    dve.wait_ge(dve_f.sem, dve_f.done(ra.b, ("sum", ST - 1), 2))
                    src = bank(5).rearrange("p (t h d) -> p t h d", t=ST, h=2)
                    nc.vector.tensor_tensor(att[ra.par][:, :, 2 * p:2 * p + 2, :], src,
                                            rden[:, :, 2 * p:2 * p + 2].unsqueeze(3).to_broadcast([P, ST, 2, DH]),
                                            ALU.mult).then_inc(dve_a.sem, dve_a.step(("att", p)))

                for h in range(NH + 1):
                    if ra and h < NH:
                        b = h % 2
                        dve.wait_ge(pe_a.sem, pe_a.done(ra.b, ("qk", h)))
                        dve.wait_ge(hop_loaded[b], ra.b * (64 * NH // 2) + 64 * (h // 2 + 1))
                        dve.wait_ge(pe_a.sem, pe_a.done(ra.b, ("turn", (h - 2) % NH, 2), 1 if h < 2 else 0))
                        nc.vector.tensor_tensor(scores[b], psum[:, 0:CAUSAL], hop_in[b], ALU.add).then_inc(
                            dve_a.sem, dve_a.step(("add", h)))
                    if rp and 1 <= h <= ST:
                        norm_query(h - 1)
                    if rp and h == 6:
                        gates_2()
                    for t in tiles:
                        if rf and ROUTE[t] == h:
                            dve.wait_ge(act_f.sem, act_f.done(rf.b, ("rstd", t)))
                            dve.wait_ge(pe_f.sem, pe_f.done(rf.b, ("turn", (t - 1) % ST), 1 if t < 1 else 0))
                            nc.vector.tensor_scalar(ffn_x, x1[t % 2], f_stats[:, 6:7], f_stats[:, 7:8], ALU.subtract,
                                                    ALU.mult).then_inc(dve_f.sem, dve_f.step(("norm", t)))
                    for t in tiles:
                        if rf and LAYER[t] == h:
                            dve.wait_ge(pool_f.sem, pool_f.done(rf.b, ("center", (t - 1) % ST), 1 if t < 1 else 0))
                            dve.wait_ge(dve_a.sem, dve_a.done(rf.b, ("att", 3)))
                            nc.vector.tensor_reduce(head_mu, att[rf.par][:, t, :, :], AX_X, ALU.add).then_inc(
                                dve_f.sem, dve_f.step(("sum", t)))
                            dve.wait_ge(dve_f.sem, dve_f.done(rf.b, ("sum", t)))
                            nc.vector.tensor_scalar(head_mu, head_mu, -1.0 / DH, None, ALU.mult).then_inc(
                                dve_f.sem, dve_f.step(("mu", t)))
                    if ra and h < NH:
                        dve.wait_ge(pool_a.sem, pool_a.done(ra.b, ("mask", h)))
                        dve.wait_ge(dve_a.sem, dve_a.done(ra.b, ("add", h)))
                        for i in range(ST):
                            part = slice(Q_OFF[i], Q_OFF[i] + P * (i + 1))
                            last = nc.vector.tensor_tensor_reduce(scores[b][:, part], scores[b][:, part],
                                                                  decay[b][:, part], 1.0, 0.0, ALU.mult, ALU.add,
                                                                  row_sum[:, i, h:h + 1])
                        last.then_inc(dve_a.sem, dve_a.step(("mul", h)))
                        if h % 2:
                            p = h // 2
                            two = slice(2 * p, 2 * p + 2)
                            dve.wait_ge(dve_a.sem, dve_a.done(ra.b, ("mul", h)))
                            dve.wait_ge(act_p.sem, act_p.done(ra.b, "stats"))
                            nc.vector.scalar_tensor_tensor(rden[:, :, two], row_sum[:, :, two], -1.0,
                                                           statT[ra.par][:, :, FG + 2 * p:FG + 2 * p + 2],
                                                           ALU.mult, ALU.max).then_inc(
                                dve_a.sem, dve_a.step(("den", p)))
                            dve.wait_ge(dve_a.sem, dve_a.done(ra.b, ("den", p)))
                            nc.vector.tensor_tensor(rden[:, :, two], rden[:, :, two], row_sum[:, :, two],
                                                    ALU.max).then_inc(dve_a.sem, dve_a.step(("abs", p)))
                            dve.wait_ge(dve_a.sem, dve_a.done(ra.b, ("abs", p)))
                            nc.vector.tensor_scalar(rden[:, :, two], rden[:, :, two], NORM_EPS, None,
                                                    ALU.add).then_inc(dve_a.sem, dve_a.step(("eps", p)))
                            dve.wait_ge(dve_a.sem, dve_a.done(ra.b, ("eps", p)))
                            nc.vector.reciprocal(rden[:, :, two], rden[:, :, two]).then_inc(
                                dve_a.sem, dve_a.step(("rden", p)))
                    for t in tiles:
                        if rf and NORM[t] == h:
                            i = t % 2
                            dve.wait_ge(pool_f.sem, pool_f.done(rf.b, ("weight", t)))
                            dve.wait_ge(pool_f.sem, pool_f.done(rf.b, ("x1_b", (t - 2) % ST), 1 if t < 2 else 0))
                            nc.vector.tensor_tensor(x1[i], att_c.rearrange("p h d -> p (h d)"), x_res[i],
                                                    ALU.add).then_inc(dve_f.sem, dve_f.step(("x1", t)))
                            dve.wait_ge(dve_f.sem, dve_f.done(rf.b, ("x1", t)))
                            nc.vector.bn_stats(f_stats[:, 0:6], x1[i]).then_inc(dve_f.sem, dve_f.step(("stats", t)))
                            dve.wait_ge(dve_f.sem, dve_f.done(rf.b, ("stats", t)))
                            stand_alone(dve, "dve")
                            nc.vector.bn_aggr(f_stats[:, 6:8], f_stats[:, 0:6]).then_inc(
                                dve_f.sem, dve_f.step(("mean", t)))
                    for t in tiles:
                        if rf and BASE[t] == h:
                            i = t % 2
                            dve.wait_ge(pe_f.sem, pe_f.done(rf.b, ("base", t)))
                            dve.wait_ge(pool_f.sem, pool_f.done(rf.b, ("x1_b", t)))
                            dve.wait_ge(out_stored[i], rf.b * 32 + 16 * (t // 2) + 32)
                            nc.vector.tensor_tensor(out_tile[i], bank(7), x1_b[i], ALU.add).then_inc(
                                dve_f.sem, dve_f.step(("out", t)))
                    if rp and h < ST:
                        stats_query(h)
                    for t in tiles:
                        if rf and LAYER[t] == h:
                            dve.wait_ge(act_f.sem, act_f.done(rf.b, ("square", t)))
                            dve.wait_ge(pool_f.sem, pool_f.done(rf.b, ("scale", (t - 1) % ST), 1 if t < 1 else 0))
                            nc.vector.tensor_reduce(head_rs, att_sq, AX_X, ALU.add).then_inc(
                                dve_f.sem, dve_f.step(("sq_sum", t)))
                    for t in tiles:
                        if rf and ROUTE[t] == h:
                            router(rf, t)
                    if ra:
                        for p in {4: [0], 6: [1], 8: [2, 3]}.get(h, []):
                            head_out(p)
                    if rp and h == 5:
                        gates_1()

            def router(rf, t):
                Z = bank(7)[:, 0:ER + E_ALL]
                mx, se, rse, den, dz, rd = (route[:, c:c + 1] for c in range(6))
                top8, where8, which = route[:, 8:16], route[:, 16:24].bitcast(U32), route[:, 24:26]
                picked, mask, weight = route[:, 28:28 + E_ALL], route[:, 40:40 + E_ALL], route[:, 52:52 + E]

                def then(name):
                    dve.wait_ge(dve_f.sem, dve_f.done(rf.b, (name, t)))

                dve.wait_ge(pe_f.sem, pe_f.done(rf.b, ("route", t)))
                nc.vector.tensor_reduce(mx, Z[:, ER:ER + E_ALL], AX_X, ALU.max).then_inc(
                    dve_f.sem, dve_f.step(("max", t)))
                then("max")
                nc.vector.tensor_scalar(logits, Z[:, ER:ER + E_ALL], mx, None, ALU.subtract).then_inc(
                    dve_f.sem, dve_f.step(("shift", t)))
                dve.wait_ge(act_f.sem, act_f.done(rf.b, ("exp", t)))
                nc.vector.reciprocal(rse, se).then_inc(dve_f.sem, dve_f.step(("rsum", t)))
                then("rsum")
                nc.vector.tensor_scalar(probs, probs, rse, None, ALU.mult).then_inc(dve_f.sem, dve_f.step(("prob", t)))
                then("prob")
                stand_alone(dve, "dve")
                nc.vector.max(top8, probs).then_inc(dve_f.sem, dve_f.step(("top", t)))
                then("top")
                stand_alone(dve, "dve")
                nc.vector.max_index(where8, top8, probs).then_inc(dve_f.sem, dve_f.step(("where", t)))
                then("where")
                nc.vector.tensor_copy(which, where8[:, 0:2]).then_inc(dve_f.sem, dve_f.step(("which", t)))
                then("which")
                nc.vector.tensor_scalar(mask, experts, which[:, 0:1], None, ALU.is_equal).then_inc(
                    dve_f.sem, dve_f.step(("first", t)))
                then("first")
                nc.vector.scalar_tensor_tensor(picked, experts, which[:, 1:2], mask, ALU.is_equal, ALU.add).then_inc(
                    dve_f.sem, dve_f.step(("both", t)))
                then("both")
                nc.vector.tensor_tensor_reduce(weight, probs[:, 0:E], picked[:, 0:E], 1.0, 0.0, ALU.mult, ALU.add,
                                               den).then_inc(dve_f.sem, dve_f.step(("pick", t)))
                then("pick")
                nc.vector.scalar_tensor_tensor(dz, den, 0.0, den, ALU.is_le, ALU.add).then_inc(
                    dve_f.sem, dve_f.step(("guard", t)))
                then("guard")
                nc.vector.reciprocal(rd, dz).then_inc(dve_f.sem, dve_f.step(("rpick", t)))
                then("rpick")
                nc.vector.tensor_scalar(weight, weight, rd, None, ALU.mult).then_inc(
                    dve_f.sem, dve_f.step(("weight", t)))
                then("weight")
                dve.wait_ge(pe_f.sem, pe_f.done(rf.b, ("mix", (t - 1) % ST), 1 if t < 1 else 0))
                nc.vector.tensor_tensor(mix.rearrange("p (e r) -> p e r", e=E),
                                        Z[:, 0:ER].rearrange("p (e r) -> p e r", e=E),
                                        weight.unsqueeze(2).to_broadcast([P, E, RANK]), ALU.mult).then_inc(
                    dve_f.sem, dve_f.step(("mix", t)))

            batch_loop(dve, run)
            all_passed(dve, "dve")

        @block.tensor
        def _(pe):
            pe_q.start(pe)
            for s in range(ST):
                pe_h[s].start(pe)
            for st in (pe_p, pe_a, pe_f):
                st.start(pe)
            pe.wait_ge(pool_setup, 2)
            pe.wait_ge(dve_setup, 8)
            for n, (srcs, rows_in, cols, dst, scale, split) in enumerate(jobs):
                if n >= 8:
                    pe.wait_ge(setup_evac, n - 7)
                for i, src in enumerate(srcs):
                    last = nc.tensor.transpose(bank(n % 8)[:, i * cols:(i + 1) * cols], src,
                                               ident[0:rows_in, 0:rows_in])
                last.then_inc(pe_setup, 1)
            pe.wait_ge(setup_evac, len(jobs))

            def queries(g):
                pe.wait_ge(dve_q.sem, dve_q.done(g, "norm"))
                pe.wait_ge(act_q.sem, act_q.done(g, "hi", 1))
                for k in range(KT):
                    last = nc.tensor.transpose(bank(0)[:, k * P:(k + 1) * P], x_norm[:, k * P:(k + 1) * P], ident)
                last.then_inc(pe_q.sem, pe_q.step("turn"))

            queries(0)

            def hop_body(s, k, last_body):
                nmt = s + 1

                def copied(g, steps):
                    for part, stages in ((0, dve_h), (1, act_h)):
                        own = [o for o in steps if evacuated_by(nmt, (o[0], o[1] % VG, *o[2:]), part)]
                        if own:
                            o = own[-1]
                            pe.wait_ge(stages[s].sem, stages[s].done(g, (o[0], o[1] % VG, *o[2:]), int(o[1] < 0)))

                for par in range(2):
                    g = k * 2 + par
                    for o in hop_order(nmt):
                        v = o[1]
                        if o[0] == "turn":
                            n = v * nmt + o[2]
                            if o[2] == 0:
                                pe.wait_ge(gathered[s][v], g * (16 * nmt) + 16 * nmt)
                            copied(g, [("turn", (n - 2) // nmt, (n - 2) % nmt)])
                            for q in range(KT):
                                last = nc.tensor.transpose(bank(1 + n % 2)[:, q * P:(q + 1) * P],
                                                           rows[v][:, o[2], q * P:(q + 1) * P], ident)
                        else:
                            if v == VG - 2 and not (last_body and par):
                                queries(g + (SEG_GROUPS * s + 1))
                            if v == 0:
                                pe.wait_ge(act_q.sem, act_q.done(g, "hi") + SEG_GROUPS * s * act_q.n)
                            copied(g, [("prod", v - 2)] + [("turn", v, t) for t in range(nmt)])
                            qd = q_diag[par].rearrange("p (k v n) -> p k v n", k=KT, v=VG)
                            for i in range(2):
                                for j in range(2):
                                    last = nc.tensor.matmul(
                                        psum[j * 64:(j + 1) * 64,
                                             (3 + 2 * (v % 2) + i) * BANK:(3 + 2 * (v % 2) + i) * BANK + P * nmt],
                                        qd[:, 2 * i + j, v, :], rowsT[v % 2][:, 2 * i + j, 0:P * nmt],
                                        start=True, stop=True)
                        last.then_inc(pe_h[s].sem, pe_h[s].step(o))

            hop_segments(pe, hop_body)
            hops_over(pe)
            pe.wait_ge(dve_setup, 9)

            def run(rp, ra, rf):
                def prepare(what, t):
                    if what == "x":
                        pe.wait_ge(dve_p.sem, dve_p.done(rp.b, ("norm", t)))
                        before = ("x", t - 1) if t else "stats"
                        pe.wait_ge(act_p.sem, act_p.done(rp.b, before, 0 if t else 1))
                        src = xq_norm
                    else:
                        if t == 0:
                            pe.wait_ge(ctx_loaded[rp.par], rp.half * 16 + 16)
                        pe.wait_ge(act_p.sem, act_p.done(rp.b, ("c", t - 1) if t else ("x", ST - 1)))
                        src = ctx_raw[rp.par][:, t, :]
                    for k in range(KT):
                        last = nc.tensor.transpose(bank(6)[:, k * P:(k + 1) * P], src[:, k * P:(k + 1) * P], ident)
                    last.then_inc(pe_p.sem, pe_p.step((what, t)))

                def gates():
                    pe.wait_ge(act_p.sem, act_p.done(rp.b, ("c", ST - 1)))
                    n = 0
                    for w, src in ((gate_qT, qT), (gate_cT, kT[rp.par])):
                        for k in range(KT):
                            last = nc.tensor.matmul(bank(6)[0:GR, :], w[:, k, :], src[:, k, :],
                                                    start=(n == 0), stop=(n == 2 * KT - 1))
                            n += 1
                    last.then_inc(pe_p.sem, pe_p.step("gates"))

                def gate_stats():
                    pe.wait_ge(dve_p.sem, dve_p.done(rp.b, "maxlog"))
                    pe.wait_ge(act_p.sem, act_p.done(rp.b, "floor"))
                    for t in tiles:
                        last = nc.tensor.transpose(bank(6)[:, t * P:(t + 1) * P], g_rows[:, t * P:(t + 1) * P], ident)
                    last.then_inc(pe_p.sem, pe_p.step("stats"))

                def values(p):
                    for h in (2 * p, 2 * p + 1):
                        pe.wait_ge(act_a.sem, act_a.done(ra.b, ("turn", h, 2)))
                    pe.wait_ge(dve_a.sem, dve_a.done(ra.b, ("att", (p - 1) % 4), 1 if p < 1 else 0))
                    for j in range(ST):
                        for e in range(2):
                            h = 2 * p + e
                            last = nc.tensor.matmul(
                                psum[e * DH:(e + 1) * DH, 5 * BANK + P * j:6 * BANK],
                                ctx_raw[ra.par][:, j, h * DH:(h + 1) * DH],
                                scoresT[h % 3][:, K_OFF[j]:K_OFF[j] + P * (ST - j)],
                                start=(j == 0), stop=(j == ST - 1), skip_group_check=True)
                    last.then_inc(pe_a.sem, pe_a.step(("pv", p)))

                def values_back(p):
                    pe.wait_ge(act_a.sem, act_a.done(ra.b, ("att", p)))
                    for i in range(ST):
                        last = nc.tensor.transpose(bank(5)[:, i * P:(i + 1) * P], attT[:, i * P:(i + 1) * P], ident)
                    last.then_inc(pe_a.sem, pe_a.step(("back", p)))

                for h in range(NH + 1):
                    if ra and h < NH:
                        pe.wait_ge(dve_a.sem, dve_a.done(ra.b, ("add", (h - 1) % NH), 1 if h < 1 else 0))
                        pe.wait_ge(pool_p.sem, pool_p.done(ra.b, ("pad", h // 2)))
                        if h == 0:
                            pe.wait_ge(act_p.sem, act_p.done(ra.b, ("c", ST - 1)))
                        for i in range(ST):
                            last = nc.tensor.matmul(psum[:, Q_OFF[i]:Q_OFF[i] + P * (i + 1)],
                                                    q_padT[:, h // 2, h % 2, i * P:(i + 1) * P],
                                                    kT[ra.par][:, h // 2, 0:P * (i + 1)], start=True, stop=True)
                        last.then_inc(pe_a.sem, pe_a.step(("qk", h)))
                    if ra and h == NH:
                        values_back(2)
                    if ra and h:
                        g = h - 1
                        for n, group in enumerate(K_BANKS):
                            pe.wait_ge(dve_a.sem, dve_a.done(ra.b, ("mul", g)))
                            before = 3 * g + n - 2
                            pe.wait_ge(act_a.sem, act_a.done(ra.b, ("turn", before // 3 % NH, before % 3),
                                                             1 if before < 0 else 0))
                            at = 0
                            for j in group:
                                for i in range(j, ST):
                                    last = nc.tensor.transpose(
                                        bank(3 + (3 * g + n) % 2)[:, at:at + P],
                                        scores[g % 2][:, Q_OFF[i] + P * j:Q_OFF[i] + P * (j + 1)], ident)
                                    at += P
                            last.then_inc(pe_a.sem, pe_a.step(("turn", g, n)))
                    for t in tiles:
                        if rf and BASE[t] == h:
                            pe.wait_ge(dve_f.sem, dve_f.done(rf.b, ("mix", t)))
                            nc.tensor.transpose(bank(7)[:, 0:P], mix, ident).then_inc(pe_f.sem, pe_f.step(("mix", t)))
                            pe.wait_ge(act_f.sem, act_f.done(rf.b, ("mixT", t)))
                            for k in range(KT):
                                nc.tensor.matmul(bank(7), ffn_xT[:, k, :], base_wT[:, k, :], start=(k == 0), stop=False)
                            nc.tensor.matmul(bank(7), mixT, lora_bT, start=False, stop=True).then_inc(
                                pe_f.sem, pe_f.step(("base", t)))
                    if rp and h == 7:
                        gate_stats()
                    for t in tiles:
                        if rf and ROUTE[t] == h:
                            pe.wait_ge(dve_f.sem, dve_f.done(rf.b, ("norm", t)))
                            pe.wait_ge(dve_f.sem, dve_f.done(rf.b, ("out", (t - 1) % ST), 1 if t < 1 else 0))
                            for k in range(KT):
                                last = nc.tensor.transpose(bank(7)[:, k * P:(k + 1) * P],
                                                           ffn_x[:, k * P:(k + 1) * P], ident)
                            last.then_inc(pe_f.sem, pe_f.step(("turn", t)))
                    if rp and 1 <= h <= ST:
                        prepare("x", h - 1)
                    if rp and h == 4:
                        prepare("c", 0)
                        prepare("c", 1)
                    if rp and h == 5:
                        prepare("c", 2)
                        prepare("c", 3)
                        gates()
                    if ra:
                        if h in (3, 5, 7):
                            values((h - 3) // 2)
                        if h in (4, 6):
                            values_back((h - 4) // 2)
                    if ra and h == NH:
                        values(3)
                        values_back(3)
                    for t in tiles:
                        if rf and ROUTE[t] == h:
                            pe.wait_ge(act_f.sem, act_f.done(rf.b, ("xT", t)))
                            pe.wait_ge(dve_f.sem, dve_f.done(rf.b, ("mix", (t - 1) % ST), 1 if t < 1 else 0))
                            for k in range(KT):
                                last = nc.tensor.matmul(bank(7)[:, 0:ER + E_ALL], ffn_xT[:, k, :],
                                                        route_wT[:, k, :], start=(k == 0), stop=(k == KT - 1))
                            last.then_inc(pe_f.sem, pe_f.step(("route", t)))

            batch_loop(pe, run)


_INS = ['x', 'ctx_1024', 'itok_SxS2_0_2016', 'L0_xattn_igate_w', 'L0_xattn_igate_b', 'L0_xattn_fgate_w',
        'L0_xattn_fgate_b', 'L0_xattn_rpe', 'L0_xattn_ln_w', 'L0_xattn_ln_b', 'L0_ffn_base_w', 'L0_ffn_base_b',
        'L0_ffn_gate_w', 'L0_ffn_lora_A', 'L0_ffn_lora_B']
_OUTS = [((32, 512, 512), 'float32')]


def kernel(**inputs):
    import numpy as _np
    import concourse.bacc as _bacc
    from concourse import mybir as _mybir
    from concourse.bass_utils import run_bass_kernel_spmd as _run

    nc = _bacc.Bacc("TRN2", target_bir_lowering=False, num_devices=1)
    arrays, args = {}, []
    for name in _INS:
        a = _np.ascontiguousarray(inputs[name])
        arrays[f"in_{name}_dram"] = a
        args.append(nc.dram_tensor(f"in_{name}_dram", a.shape, _mybir.dt.from_np(a.dtype), kind="ExternalInput").ap())
    for i, (shape, dtype) in enumerate(_OUTS):
        dt = _mybir.dt.from_np(_np.dtype(dtype))
        args.append(nc.dram_tensor(f"out_{i}_dram", shape, dt, kind="ExternalOutput").ap())
    build(nc, *args)
    r = _run(nc, [arrays], core_ids=[0])
    return r.results[0]["out_0_dram"]
```
